# Optimizing a Trainium2 kernel written in Bass

```python
import numpy as np
import jax
import jax.numpy as jnp

def _softmax(x, axis=-1):
    return jax.nn.softmax(x, axis=axis)

def _gelu(x):
    return jax.nn.gelu(x, approximate=True)

def _silu(x):
    return jax.nn.silu(x)

def _sigmoid(x):
    return jax.nn.sigmoid(x)

def _layernorm(x, axis=-1, eps=1e-05):
    m = jnp.mean(x, axis=axis, keepdims=True)
    v = jnp.var(x, axis=axis, keepdims=True)
    return (x - m) / jnp.sqrt(v + eps)

def _scatter_add(tgt, idx, src, axis=0):
    return tgt.at[idx].add(src)

def _segment_sum(src, seg, n):
    return jax.ops.segment_sum(src, seg, n)
kernel_name = 'mk_gnn_preln_d1_gnn_r8_f3540e'

def setup_inputs(seed: int=0):
    np.random.seed(seed)
    _w = jnp.asarray

    def _rec_inputs():
        import jax
        import jax.numpy as jnp
        _gk = jax.random.key(seed)
        x = -0.0003713 + 1 * jax.random.normal(jax.random.fold_in(_gk, 1), (12500, 128), jnp.float32)
        _s = jax.random.randint(jax.random.fold_in(_gk, 2), (100000,), 0, 12500, jnp.int32)
        _d = jax.random.randint(jax.random.fold_in(_gk, 3), (100000,), 0, 12500, jnp.int32)
        _loop = jnp.arange(12500, dtype=jnp.int32)
        src = jnp.concatenate([_s, _d, _loop])
        dst = jnp.concatenate([_d, _s, _loop])
        _o = jnp.argsort(dst, stable=True)
        src = src[_o]
        dst = dst[_o]
        edge_type_16 = jax.random.randint(jax.random.fold_in(_gk, 12), (212500,), 0, 16, jnp.int32)
        return (x, src, dst, edge_type_16)
    x, src, dst, edge_type_16 = _rec_inputs()

    def _L0_gnn_setup():
        import jax, jax.numpy as jnp
        import numpy as np
        N_NODES = 12500
        N_EDGES = 400000
        IN_FEAT = 128
        OUT_FEAT = 128
        NUM_RELS = 16
        NUM_BASES = 8
        key = jax.random.key(seed)
        ks = jax.random.split(key, 7)
        x = jax.random.normal(ks[0], (N_NODES, IN_FEAT), dtype=jnp.float32)
        src = jax.random.randint(ks[1], (N_EDGES,), 0, N_NODES, dtype=jnp.int64)
        dst = jax.random.randint(ks[2], (N_EDGES,), 0, N_NODES, dtype=jnp.int64)
        etypes = jax.random.randint(ks[3], (N_EDGES,), 0, NUM_RELS, dtype=jnp.int64)
        gain = float(np.sqrt(2.0))
        limit_w = gain * float(np.sqrt(6.0 / (IN_FEAT + OUT_FEAT)))
        weight = jax.random.uniform(ks[4], (NUM_BASES, IN_FEAT, OUT_FEAT), dtype=jnp.float32, minval=-limit_w, maxval=limit_w)
        limit_c = float(np.sqrt(6.0 / (NUM_RELS + NUM_BASES)))
        w_comp = jax.random.uniform(ks[5], (NUM_RELS, NUM_BASES), dtype=jnp.float32, minval=-limit_c, maxval=limit_c)
        h_bias = jnp.zeros((OUT_FEAT,), dtype=jnp.float32)
        return {'x': x, 'weight': weight, 'w_comp': w_comp, 'h_bias': h_bias, 'src': src, 'dst': dst, 'etypes': etypes}
    _L0_gnn_all = _L0_gnn_setup()
    _L0_gnn_in = {k: v for k, v in _L0_gnn_all.items() if k in ('weight', 'w_comp', 'h_bias')}
    del _L0_gnn_all
    return {'x': x, 'src': src, 'dst': dst, 'edge_type_16': edge_type_16, 'L0_gnn_weight': _L0_gnn_in['weight'], 'L0_gnn_w_comp': _L0_gnn_in['w_comp'], 'L0_gnn_h_bias': _L0_gnn_in['h_bias']}

def reference(x, src, dst, edge_type_16, L0_gnn_weight, L0_gnn_w_comp, L0_gnn_h_bias):
    import jax
    import jax.numpy as jnp

    def _L0_gnn_ref(x, weight, w_comp, h_bias, src, dst, etypes):
        import jax, jax.numpy as jnp
        import numpy as np
        N_NODES = 12500
        N_EDGES = 400000
        IN_FEAT = 128
        OUT_FEAT = 128
        NUM_RELS = 16
        NUM_BASES = 8
        W = jnp.einsum('rb,bio->rio', w_comp, weight)
        h = jnp.einsum('ni,rio->rno', x, W)
        msg = h[etypes, src]
        node_repr = jax.ops.segment_sum(msg, dst, num_segments=N_NODES)
        node_repr = node_repr + h_bias
        return node_repr
    h = jnp.maximum(_layernorm(x, axis=-1), 0.0)
    x = x + _L0_gnn_ref(h, L0_gnn_weight, L0_gnn_w_comp, L0_gnn_h_bias, src, dst, edge_type_16)
    return x

_drawn_inputs = setup_inputs


def setup_inputs(seed=0):
    import zlib

    import numpy as np

    out = dict(_drawn_inputs(seed))
    spreads = {'L0_gnn_h_bias': (0.0, 0.313)}
    factors = {}
    for name, (base, spread) in spreads.items():
        noise = np.random.default_rng([zlib.crc32(name.encode()), seed]).standard_normal(out[name].shape)
        drawn = base * np.exp(spread * noise) if base else spread * noise
        out[name] = jnp.asarray(drawn.astype(out[name].dtype))
    for name, factor in factors.items():
        out[name] = (out[name] * factor).astype(out[name].dtype)
    return out
```

```python
import concourse.bass as bass
from concourse import mybir
from contextlib import ExitStack



def gnn_kernel(nc, x, src, dst, etype, weight, w_comp, h_bias, out):
    F32 = mybir.dt.float32
    I32 = mybir.dt.int32
    ALU = mybir.AluOpType
    ACT = mybir.ActivationFunctionType
    AX = mybir.AxisListType

    P = 128
    N, D = x.shape
    E = src.shape[0]
    B = weight.shape[0]
    R = w_comp.shape[0]
    EPS = 1e-5
    DVE_ROWS = 3

    TILES = -(-E // P)
    BLOCKS = -(-TILES // P)
    TG = 15
    GROUPS = -(-TILES // TG)
    LAST_TILES = TILES - (GROUPS - 1) * TG
    FULL = GROUPS - 1
    SPAN = 13
    KEYS = SPAN * R
    WIN = P + SPAN
    EARLY = 4
    assert FULL % 2 == 0 and EARLY % 2 == 0
    MIX_TILES = 9
    AHEAD = 3
    IDX_A = 8
    W_BANKS = R * D // 512
    CHECK_PAIR = 20
    Q = 4
    DQ = D // Q
    PAD = float(1 << 20)

    ROWS = N // P
    MAIN = ROWS * P
    REST = N - MAIN
    CH = 16
    CHUNKS = [(c, min(c + CH, ROWS)) for c in range(0, ROWS - ROWS % CH, CH)]
    if ROWS % CH:
        if ROWS % CH < 4:
            CHUNKS[-1] = (CHUNKS[-1][0], ROWS)
        else:
            CHUNKS.append((ROWS - ROWS % CH, ROWS))
    TABLE_CH = len(CHUNKS) + 1
    STAT_ROWS = ROWS + 1 + EARLY * TG

    FB = (BLOCKS - 1) * P * P
    TAIL_T = (E - FB) // P
    TAIL_E = E - FB - TAIL_T * P

    h_dram = nc.dram_tensor("h_table", (N, D), F32).ap()
    offs_dram = nc.dram_tensor("offs_scratch", (GROUPS, 16), I32).ap()
    base_dram = nc.dram_tensor("base_scratch", (GROUPS, 1), I32).ap()

    with ExitStack() as ctx:
        def sb(name, shape, dt=F32):
            return ctx.enter_context(nc.sbuf_tensor(name, shape, dt))

        def sem(name):
            return ctx.enter_context(nc.semaphore(name))

        xh = sb("xh", [P, ROWS, D])
        xr = sb("xr", [P, D])
        stats = sb("stats", [P, STAT_ROWS, 6])
        mean2 = sb("mean2", [P, STAT_ROWS])
        mdiff = sb("mdiff", [P, STAT_ROWS])
        var = sb("var", [P, STAT_ROWS])
        std = sb("std", [P, STAT_ROWS])
        rstd = sb("rstd", [P, STAT_ROWS])
        shift = sb("shift", [P, STAT_ROWS])
        eps_c = sb("eps_c", [P, 1])

        src_i = sb("src_i", [P, BLOCKS, P], I32)
        dst_i = sb("dst_i", [P, BLOCKS, P], I32)
        nxt_i = sb("nxt_i", [P, BLOCKS, P], I32)
        typ_i = sb("typ_i", [P, BLOCKS, P], I32)
        rel = sb("rel", [P, BLOCKS, P])
        key = sb("key", [P, BLOCKS, P])
        src_t = sb("src_t", [P, BLOCKS * P + TG], I32)
        key_t = sb("key_t", [P, BLOCKS * P])

        first_i = sb("first_i", [GROUPS, 16], I32)
        offs_f = sb("offs_f", [GROUPS, 16])
        offs_i = sb("offs_i", [GROUPS, 16], I32)
        base_i = sb("base_i", [GROUPS, 1], I32)
        offs_row = sb("offs_row", [1, GROUPS * 16], I32)
        base_row = sb("base_row", [1, GROUPS], I32)
        last_i = sb("last_i", [P, 1], I32)
        node_f = sb("node_f", [P, 1])
        part_f = sb("part_f", [P, 1])
        last_idx = sb("last_idx", [P, 1], I32)
        ident = sb("ident", [P, P])
        keys_iota = sb("keys_iota", [P, SPAN, R + 1])
        zeros = sb("zeros", [P, R])

        wt = sb("wt", [Q * B, D, DQ])
        wc_q = sb("wc_q", [Q * B, Q, R])
        W = sb("W", [P, R, D])
        bias_bc = sb("bias_bc", [P, D])

        idx = sb("idx", [P, TG], I32)
        G = sb("G", [P, TG, D])
        G_early = sb("G_early", [P, EARLY, TG, D])
        onehot = sb("onehot", [P, AHEAD, KEYS])
        agg = sb("agg", [P, 2, WIN, R])
        x_t = sb("x_t", [P, 2, D])
        x_last = sb("x_last", [P, D])
        out_sb = sb("out_sb", [P, 2, D])

        excess = sb("excess", [P, 5])
        excess_max = sb("excess_max", [P, 1])
        flag_f = sb("flag_f", [1, 1])
        flag_i = sb("flag_i", [1, 1], I32)

        picked = xh[:, 0:R, :]
        sums = xh[:, R:2 * R, :]
        same = xh[:, 2 * R, :]
        before = xh[:, 2 * R + 1, :]
        twins = xh[:, 2 * R + 2, :]
        h_rows = xh[:, 2 * R + 3, :]
        out_rows = xh[:, 2 * R + 4, :]
        new_rows = xh[:, 2 * R + 5, :]
        places = xh[:, 2 * R + 6, :]
        typ_onehot = xh[:, 2 * R + 7, 0:R]
        dst_f = xh[:, 2 * R + 8, 0:1]
        typ_f = xh[:, 2 * R + 8, 1:2]
        twins_f = xh[:, 2 * R + 8, 2:3]
        skip_f = xh[:, 2 * R + 8, 3:4]
        dst_row = dst_i[:, 0, :]
        dst_col = typ_i[:, 0, 0:1]
        src_col = typ_i[:, 0, 1:2]
        typ_col = typ_i[:, 0, 2:3]
        target = typ_i[:, 0, 3:4]

        def bank(name):
            return ctx.enter_context(nc.psum_tensor(name, [P, 512], F32))

        prod = [bank(f"prod{i}") for i in range(AHEAD)]
        mix = [bank(f"mix{i}") for i in range(2)]
        flag_bank = bank("flag_bank")
        sum_banks = prod + [flag_bank]
        turn = [bank(f"turn{i}") for i in range(2)]
        w_banks = mix + turn

        x_in = [sem(f"x_in{i}") for i in range(TABLE_CH)]
        src_in = sem("src_in")
        dst_in = sem("dst_in")
        typ_in = sem("typ_in")
        first_in = sem("first_in")
        w_in = sem("w_in")
        bias_in = sem("bias_in")
        pads_set = sem("pads_set")
        consts_set = sem("consts_set")
        dve_step = sem("dve_step")
        pool_step = sem("pool_step")
        var_ready = sem("var_ready")
        std_ready = sem("std_ready")
        norm_ready = sem("norm_ready")
        h_ready = sem("h_ready")
        h_dve_ready = sem("h_dve_ready")
        h_stored = sem("h_stored")
        offs_ready = sem("offs_ready")
        offs_stored = sem("offs_stored")
        rows_in = sem("rows_in")
        key_ready = sem("key_ready")
        srcf_ready = sem("srcf_ready")
        turned = sem("turned")
        unturned = sem("unturned")
        w_turned = sem("w_turned")
        w_ready = sem("w_ready")
        idx_seen = sem("idx_seen")
        checks_ready = sem("checks_ready")
        window_ready = sem("window_ready")
        out_free = sem("out_free")
        x_last_in = sem("x_last_in")
        idx_ready = [sem("idx_ready_a"), sem("idx_ready_b")]
        early_in = [sem(f"early_in{g}") for g in range(EARLY)]
        gathered = [sem(f"gathered{j}") for j in range(TG)]
        onehot_ready = sem("onehot_ready")
        prod_ready = sem("prod_ready")
        prod_free = sem("prod_free")
        agg_zeroed = sem("agg_zeroed")
        xt_in = [sem("xt_in0"), sem("xt_in1")]
        mixed = sem("mixed")
        out_ready = sem("out_ready")
        out_stored = sem("out_stored")
        last_in = sem("last_in")
        nxt_in = sem("nxt_in")
        last_idx_ready = sem("last_idx_ready")
        last_stored = sem("last_stored")
        excess_ready = sem("excess_ready")
        excess_turned = sem("excess_turned")
        flag_ready = sem("flag_ready")
        general_x_in = sem("general_x_in")
        general_dve = sem("general_dve")
        general_biased = sem("general_biased")
        general_based = sem("general_based")
        general_consts = sem("general_consts")
        general_seen = sem("general_seen")
        edges_in = sem("edges_in")
        rows_gathered = sem("rows_gathered")
        picked_ready = sem("picked_ready")
        target_ready = sem("target_ready")
        sums_ready = sem("sums_ready")
        sums_moved = sem("sums_moved")
        new_rows_ready = sem("new_rows_ready")
        new_rows_moved = sem("new_rows_moved")
        rows_scattered = sem("rows_scattered")

        block = ctx.enter_context(nc.Block())

        def edge_loads(eng, a, tile, done, skip=0):
            a = a[skip:E] if skip else a
            eng.dma_start(tile[:, 0:BLOCKS - 1, :],
                          a[0:FB].rearrange("(b p e) -> p b e", p=P, e=P)).then_inc(done, 16)
            eng.dma_start(tile[0:TAIL_T, BLOCKS - 1, :],
                          a[FB:FB + TAIL_T * P].rearrange("(p e) -> p e", e=P)).then_inc(done, 16)
            eng.dma_start(tile[TAIL_T:TAIL_T + 1, BLOCKS - 1, 0:TAIL_E - skip],
                          a[FB + TAIL_T * P:E - skip].rearrange("(p e) -> p e", p=1)).then_inc(done, 16)

        def x_chunk(c):
            if c == TABLE_CH - 1:
                return xr[0:REST, :], x[MAIN:N, :], h_dram[MAIN:N, :]
            a, b = CHUNKS[c]
            xv = x[0:MAIN, :].rearrange("(p r) d -> p r d", p=P)
            hv = h_dram[0:MAIN, :].rearrange("(p r) d -> p r d", p=P)
            return xh[:, a:b, :], xv[:, a:b, :], hv[:, a:b, :]

        def norm_chunk(c):
            if c >= TABLE_CH:
                g = c - TABLE_CH
                a = ROWS + 1 + g * TG
                return P, a, a + TG, lambda r: G_early[:, g, r - a, :], early_in[g], 16 * TG
            if c == TABLE_CH - 1:
                return REST, ROWS, ROWS + 1, lambda r: xr[0:REST, :], x_in[c], 16
            a, b = CHUNKS[c]
            return P, a, b, lambda r: xh[:, r, :], x_in[c], 16

        ORDER = list(range(TABLE_CH))
        ORDER[TABLE_CH - 1:TABLE_CH - 1] = [TABLE_CH + 1]
        ORDER[TABLE_CH // 2:TABLE_CH // 2] = [TABLE_CH]
        ORDER += range(TABLE_CH + 2, TABLE_CH + EARLY)
        assert ORDER[TABLE_CH + 1] == TABLE_CH - 1
        turn_of = {c: n for n, c in enumerate(ORDER)}

        def dve_rows(c):
            return DVE_ROWS if c < TABLE_CH - 1 else 0

        def batches():
            return [list(range(b, min(b + 4, BLOCKS))) for b in range(0, BLOCKS, 4)]

        def general_path(eng):
            eng.wait_ge(flag_ready, 1)
            return eng.If(eng.value_load(flag_i[0:1, 0:1], min_val=0, max_val=1) > 0)

        def general_tiles(eng, tile):
            with eng.Fori(0, TILES - 1) as t:
                tile(t, P)
            tile(TILES - 1, TAIL_E)

        @block.sync
        def _(sp):
            sp.wait_ge(pads_set, 6)
            edge_loads(sp, src, src_i, src_in)
            edge_loads(sp, dst, dst_i, dst_in)
            edge_loads(sp, etype, typ_i, typ_in)
            sp.dma_start(first_i[0:FULL, 0:TG], dst[0:FULL * TG * P].rearrange(
                "(g i e) -> g i e", i=TG, e=P)[:, :, 0], allow_slow_non_contiguous=True).then_inc(first_in, 16)
            sp.dma_start(first_i[0:FULL, TG:TG + 1], dst[TG * P:TG * P * FULL + 1:TG * P].rearrange(
                "(g i) -> g i", i=1), allow_slow_non_contiguous=True).then_inc(first_in, 16)
            sp.dma_start(first_i[FULL:GROUPS, 0:LAST_TILES], dst[FULL * TG * P:E:P].rearrange(
                "(g i) -> g i", g=1), allow_slow_non_contiguous=True).then_inc(first_in, 16)
            sp.dma_start(last_i[:, :], dst[FULL * TG * P:FULL * TG * P + 1].partition_broadcast(P)
                          ).then_inc(last_in, 16)
            for c in range(TABLE_CH):
                dstn, srcn, _ = x_chunk(c)
                sp.dma_start(dstn, srcn).then_inc(x_in[c], 16)
            for q in range(Q):
                rows = slice(q * B, (q + 1) * B)
                sp.dma_start(wt[rows, :, :], weight[:, :, q * DQ:(q + 1) * DQ]).then_inc(w_in, 16)
                sp.dma_start(wc_q[rows, q, :], w_comp.rearrange("r b -> b r"), allow_slow_non_contiguous=True
                              ).then_inc(w_in, 16)
            sp.dma_start(bias_bc[:, :], h_bias.partition_broadcast(P)).then_inc(bias_in, 16)
            sp.sem_inc(out_free, 2)
            sp.wait_ge(offs_ready, 2)
            sp.dma_start(offs_dram[:, :], offs_i[:, :]).then_inc(offs_stored, 16)
            sp.dma_start(base_dram[:, :], base_i[:, :]).then_inc(offs_stored, 16)
            sp.wait_ge(offs_stored, 32)
            sp.dma_start(offs_row[:, :], offs_dram.rearrange("(a g) i -> a (g i)", a=1)).then_inc(rows_in, 16)
            sp.dma_start(base_row[:, :], base_dram.rearrange("(a g) i -> a (g i)", a=1)).then_inc(rows_in, 16)
            for c in range(TABLE_CH):
                srcn, _, dstn = x_chunk(c)
                if dve_rows(c):
                    sp.wait_ge(h_dve_ready, c + 1)
                sp.wait_ge(h_ready, turn_of[c] + 1)
                sp.dma_start(dstn, srcn).then_inc(h_stored, 16)
            edge_loads(sp, dst, nxt_i, nxt_in, skip=1)
            sp.wait_ge(rows_in, 32)
            with sp.Fori(0, FULL // 2) as gg:
                for par in range(2):
                    g = gg * 2 + par
                    base = sp.value_load(base_row[0:1, bass.ds(g, 1)], min_val=0, max_val=N - P)
                    sp.dma_start(x_t[:, par, :], x[bass.ds(base, P), :]).then_inc(xt_in[par], 16)
                    sp.wait_ge(out_ready, g + 1)
                    sp.dma_start(out[bass.ds(base, P), :], out_sb[:, par, :]).then_inc(out_stored, 16)
                    sp.wait_ge(out_stored, (g + 1) * 16)
                    sp.sem_inc(out_free, 1)

            with general_path(sp):
                sp.wait_ge(h_stored, 16 * TABLE_CH)
                sp.wait_ge(last_stored, 16)
                sp.dma_start(xh[:, :, :], x[0:MAIN, :].rearrange("(p r) d -> p r d", p=P)).then_inc(general_x_in, 16)
                sp.dma_start(xr[0:REST, :], x[MAIN:N, :]).then_inc(general_x_in, 16)
                sp.wait_ge(general_biased, 2)
                sp.dma_start(out[0:MAIN, :].rearrange("(p r) d -> p r d", p=P), xh[:, :, :]).then_inc(general_based, 16)
                sp.dma_start(out[MAIN:N, :], xr[0:REST, :]).then_inc(general_based, 16)
                sp.wait_ge(general_based, 32)

                def tile(t, n):
                    edges = bass.ds(t * P, n)
                    for col, a in ((dst_col, dst), (src_col, src), (typ_col, etype)):
                        sp.dma_start(col[0:n, :], a[edges].rearrange("(p o) -> p o", o=1),
                                     allow_slow_non_contiguous=True).then_inc(edges_in, 16)
                    sp.dma_start(dst_row[0:n, 0:n], dst[edges].partition_broadcast(n)).then_inc(edges_in, 16)
                    sp.wait_ge(rows_scattered, 16 * (t + 1))
                    sp.sem_inc(general_seen, 1)

                general_tiles(sp, tile)

        @block.gpsimd
        def _(pool):
            pool.memset(src_i[:, BLOCKS - 1, :], 0).then_inc(pads_set, 1)
            pool.memset(dst_i[:, BLOCKS - 1, :], int(PAD)).then_inc(pads_set, 1)
            pool.memset(nxt_i[:, BLOCKS - 1, :], int(PAD)).then_inc(pads_set, 1)
            pool.memset(typ_i[:, BLOCKS - 1, :], 0).then_inc(pads_set, 1)
            pool.memset(first_i[:, :], int(PAD)).then_inc(pads_set, 1)
            pool.memset(wc_q[:, :, :], 0.0).then_inc(pads_set, 1)
            pool.memset(ident[:, :], 0.0).then_inc(pool_step, 1)
            pool.wait_ge(pool_step, 1)
            pool.affine_select(out=ident[:, :], in_=ident[:, :], compare_op=ALU.not_equal, fill=1.0,
                               base=0, pattern=[[-1, P]], channel_multiplier=1).then_inc(consts_set, 1)
            pool.iota(keys_iota[:, :, :], pattern=[[R, SPAN], [1, R + 1]], base=0, channel_multiplier=0,
                      allow_small_or_imprecise_dtypes=True).then_inc(consts_set, 1)
            pool.iota(part_f[:, :], pattern=[[0, 1]], base=0, channel_multiplier=1,
                      allow_small_or_imprecise_dtypes=True).then_inc(consts_set, 1)
            pool.memset(zeros[:, :], 0.0).then_inc(consts_set, 1)
            pool.memset(eps_c[:, :], EPS).then_inc(consts_set, 1)
            pool.memset(src_t[:, BLOCKS * P:], 0).then_inc(consts_set, 1)
            pool.memset(x_last[:, :], 0.0).then_inc(pool_step, 1)
            pool.wait_ge(unturned, 1)
            for g in range(EARLY):
                for j in range(TG):
                    t = g * TG + j
                    pool.indirect_dma_start(G_early[:, g, j, :], None, x[:, :],
                                            bass.IndirectOffsetOnAxis(ap=src_t[:, t:t + 1], axis=0)
                                            ).then_inc(early_in[g], 16)
            pool.wait_ge(last_idx_ready, 2)
            pool.wait_ge(pool_step, 2)
            pool.indirect_dma_start(x_last[:, :], None, x[:, :],
                                    bass.IndirectOffsetOnAxis(ap=last_idx[:, 0:1], axis=0),
                                    bounds_check=N - 1, oob_is_err=False).then_inc(x_last_in, 16)

            pool.wait_ge(h_stored, 16 * TABLE_CH)

            def gathers(g, tiles):
                for j in range(tiles):
                    if j == 0:
                        pool.wait_ge(idx_ready[0], g + 1)
                        pool.sem_inc(idx_seen, 1)
                    if j == IDX_A:
                        pool.wait_ge(idx_ready[1], g + 1)
                        pool.sem_inc(idx_seen, 1)
                    pool.indirect_dma_start(G[:, j, :], None, h_dram[:, :],
                                            bass.IndirectOffsetOnAxis(ap=idx[:, j:j + 1], axis=0)
                                            ).then_inc(gathered[j], 16)

            with pool.Fori(0, FULL - EARLY) as g:
                gathers(g, TG)
            gathers(FULL - EARLY, LAST_TILES)
            pool.wait_ge(out_ready, GROUPS)
            pool.wait_ge(out_stored, 16 * FULL)
            pool.indirect_dma_start(out[:, :], bass.IndirectOffsetOnAxis(ap=last_idx[:, 0:1], axis=0),
                                    out_sb[:, 0, :], None, bounds_check=N - 1,
                                    oob_is_err=False).then_inc(last_stored, 16)
            pool.wait_ge(last_stored, 16)

            with general_path(pool):
                pool.wait_ge(general_based, 32)
                pool.iota(places[:, :], pattern=[[1, P]], base=0, channel_multiplier=0,
                          allow_small_or_imprecise_dtypes=True).then_inc(general_consts, 1)

                def tile(t, n):
                    pool.wait_ge(edges_in, 64 * (t + 1))
                    pool.sem_inc(general_seen, 1)
                    pool.indirect_dma_start(h_rows[0:n, :], None, h_dram[:, :],
                                            bass.IndirectOffsetOnAxis(ap=src_col[0:n, :], axis=0)
                                            ).then_inc(rows_gathered, 16)
                    pool.indirect_dma_start(out_rows[0:n, :], None, out[:, :],
                                            bass.IndirectOffsetOnAxis(ap=dst_col[0:n, :], axis=0)
                                            ).then_inc(rows_gathered, 16)
                    pool.wait_ge(new_rows_moved, t + 1)
                    pool.wait_ge(target_ready, t + 1)
                    pool.sem_inc(general_seen, 1)
                    pool.indirect_dma_start(out[:, :], bass.IndirectOffsetOnAxis(ap=target[0:n, :], axis=0),
                                            new_rows[0:n, :], None, bounds_check=N - 1,
                                            oob_is_err=False).then_inc(rows_scattered, 16)

                general_tiles(pool, tile)
                pool.wait_ge(rows_scattered, 16 * TILES)

        @block.scalar
        def _(act):
            act.wait_ge(src_in, 48)
            act.activation(key[:, :, :], src_i[:, :, :], ACT.Copy).then_inc(srcf_ready, 1)
            act.wait_ge(consts_set, 6)
            for k, bs in enumerate(batches()):
                act.wait_ge(turned, k + 1)
                act.activation(src_t[:, bs[0] * P:(bs[-1] + 1) * P], turn[k % 2][:, 0:len(bs) * P],
                               ACT.Copy).then_inc(unturned, 1)
            act.wait_ge(unturned, len(batches()))
            for half, (a, b) in enumerate(((0, IDX_A), (IDX_A, TG))):
                act.activation(idx[:, a:b], src_t[:, EARLY * TG + a:EARLY * TG + b], ACT.Copy
                               ).then_inc(idx_ready[half], 1)
            for par in range(2):
                act.activation(agg[:, par, :, :], zeros[:, None, :].to_broadcast([P, WIN, R]),
                               ACT.Copy).then_inc(agg_zeroed, 1)

            for k, bs in enumerate(batches()):
                act.wait_ge(turned, len(batches()) + k + 1)
                act.activation(key_t[:, bs[0] * P:(bs[-1] + 1) * P],
                               turn[(k + len(batches())) % 2][:, 0:len(bs) * P], ACT.Copy).then_inc(unturned, 1)

            def place_w(k):
                n = DQ // W_BANKS
                act.wait_ge(w_turned, k + 1)
                act.activation(W[:, :, :].rearrange("p r (q o) -> p o q r", q=Q)[:, k * n:(k + 1) * n, :, :],
                               w_banks[k][:, :].rearrange("p (o q r) -> p o q r", q=Q, r=R),
                               ACT.Copy).then_inc(w_ready, 1)

            def root(c):
                parts, a, b = norm_chunk(c)[:3]
                act.wait_ge(var_ready, turn_of[c] + 1)
                act.activation(std[0:parts, a:b], var[0:parts, a:b], ACT.Sqrt,
                               bias=eps_c[0:parts, :]).then_inc(std_ready, 1)

            def relus(c):
                parts, a, b, row = norm_chunk(c)[:4]
                act.wait_ge(norm_ready, turn_of[c] + 1)
                for r in range(a, b - dve_rows(c)):
                    last = act.activation(row(r), row(r), ACT.Relu, bias=shift[0:parts, r:r + 1],
                                          scale=rstd[0:parts, r:r + 1])
                last.then_inc(h_ready, 1)

            first = ORDER[:TABLE_CH + 2]
            root(first[0])
            for n, c in enumerate(first):
                if n + 1 < len(first):
                    root(first[n + 1])
                relus(c)
            for k in range(W_BANKS):
                place_w(k)
            for c in ORDER[TABLE_CH + 2:]:
                root(c)
                relus(c)

            def evacuate(g, par):
                act.wait_ge(mixed, g + 1)
                act.wait_ge(out_free, g + 1)
                act.activation(out_sb[:, par, :], mix[par][:, 0:D], ACT.Copy).then_inc(out_ready, 1)

            def renew(g, par):
                act.wait_ge(window_ready, g + 2)
                act.activation(agg[:, par, :, :], zeros[:, None, :].to_broadcast([P, WIN, R]),
                               ACT.Copy).then_inc(agg_zeroed, 1)

            for g in range(EARLY):
                evacuate(g, g % 2)
                renew(g, g % 2)
            with act.Fori(0, (FULL - EARLY) // 2) as gg:
                for par in range(2):
                    g = gg * 2 + (EARLY + par)
                    for half, (a, b) in enumerate(((0, IDX_A), (IDX_A, TG))):
                        act.wait_ge(prod_ready, g * TG + b)
                        act.activation(idx[:, a:b], src_t[:, bass.ds((g + 1) * TG + a, b - a)],
                                       ACT.Copy).then_inc(idx_ready[half], 1)
                    evacuate(g, par)
                    renew(g, par)
            evacuate(FULL, 0)

            with general_path(act):
                def tile(t, n):
                    act.wait_ge(sums_ready, t + 1)
                    for k in range(R // 4):
                        last = act.activation(sums[:, 4 * k:4 * k + 4, 0:n],
                                              sum_banks[k][:, :].rearrange("p (r e) -> p r e", e=P)[:, :, 0:n],
                                              ACT.Copy)
                    last.then_inc(sums_moved, 1)
                    act.wait_ge(new_rows_ready, t + 1)
                    act.activation(new_rows[0:n, :], mix[0][0:n, 0:D], ACT.Copy).then_inc(new_rows_moved, 1)

                general_tiles(act, tile)

        @block.vector
        def _(dve):
            steps = [0]

            def link(instruction):
                steps[0] += 1
                instruction.then_inc(dve_step, 1)
                dve.wait_ge(dve_step, steps[0])

            def statistics(c):
                parts, a, b, row, done, count = norm_chunk(c)
                dve.wait_ge(done, count)
                for r in range(a, b):
                    last = dve.bn_stats(stats[0:parts, r, :], row(r))
                link(last)
                s = stats[0:parts, a:b, :]
                m = slice(a, b)
                dve.tensor_tensor(mean2[0:parts, m], s[:, :, 1], s[:, :, 4], ALU.add)
                dve.tensor_tensor(var[0:parts, m], s[:, :, 2], s[:, :, 5], ALU.add)
                link(dve.tensor_tensor(mdiff[0:parts, m], s[:, :, 1], s[:, :, 4], ALU.subtract))
                link(dve.scalar_tensor_tensor(out=mdiff[0:parts, m], in0=mdiff[0:parts, m], scalar=0.25,
                                              in1=mdiff[0:parts, m], op0=ALU.mult, op1=ALU.mult))
                dve.scalar_tensor_tensor(out=var[0:parts, m], in0=var[0:parts, m], scalar=1.0 / D,
                                         in1=mdiff[0:parts, m], op0=ALU.mult, op1=ALU.add
                                         ).then_inc(var_ready, 1)

            def scales(c):
                parts, a, b, row = norm_chunk(c)[:4]
                dve.wait_ge(std_ready, turn_of[c] + 1)
                link(dve.reciprocal(rstd[0:parts, a:b], std[0:parts, a:b]))
                dve.scalar_tensor_tensor(out=shift[0:parts, a:b], in0=mean2[0:parts, a:b], scalar=-0.5,
                                         in1=rstd[0:parts, a:b], op0=ALU.mult, op1=ALU.mult
                                         ).then_inc(norm_ready, 1)
                if dve_rows(c):
                    dve.wait_ge(norm_ready, turn_of[c] + 1)
                    for r in range(b - dve_rows(c), b):
                        last = dve.tensor_scalar(row(r), row(r), rstd[0:parts, r:r + 1], shift[0:parts, r:r + 1],
                                                 ALU.mult, ALU.add)
                    link(last)
                    rows = xh[:, b - dve_rows(c):b, :]
                    dve.tensor_scalar(rows, rows, 0.0, None, ALU.max).then_inc(h_dve_ready, 1)

            dve.wait_ge(dst_in, 48)
            link(dve.tensor_tensor(rel[:, :, :], dst_i[:, :, :], dst_i[:, :, 0:1].to_broadcast([P, BLOCKS, P]),
                                   ALU.subtract))
            dve.wait_ge(typ_in, 48)
            dve.wait_ge(turned, len(batches()))
            dve.scalar_tensor_tensor(out=key[:, :, :], in0=rel[:, :, :], scalar=float(R), in1=typ_i[:, :, :],
                                     op0=ALU.mult, op1=ALU.add).then_inc(key_ready, 1)

            dve.wait_ge(last_in, 16)
            dve.wait_ge(consts_set, 6)
            dve.tensor_tensor(last_idx[:, :], last_i[:, :], part_f[:, :], ALU.add).then_inc(last_idx_ready, 2)
            dve.wait_ge(first_in, 48)
            link(dve.memset(first_i[0:1, 0:1], 0))
            link(dve.tensor_scalar(offs_f[:, :], first_i[:, :], first_i[:, 0:1], float(P - 1),
                                   ALU.subtract, ALU.min))
            dve.tensor_scalar(offs_i[:, :], offs_f[:, :], 0.0, None, ALU.max).then_inc(offs_ready, 1)
            dve.tensor_scalar(base_i[:, :], first_i[:, 0:1], float(N - P), None, ALU.min).then_inc(offs_ready, 1)

            first = ORDER[:TABLE_CH + 2]
            for n, c in enumerate(first):
                statistics(c)
                if n >= 1:
                    scales(first[n - 1])
            scales(first[-1])

            def make_onehot(t, slot):
                dve.tensor_scalar(onehot[:, slot, :], keys_iota[:, :, 0:R], key_t[:, bass.ds(t, 1)], None,
                                  ALU.is_equal).then_inc(onehot_ready, 1)

            dve.wait_ge(unturned, 2 * len(batches()))
            for t in range(AHEAD):
                make_onehot(t, t)
            dve.memset(stats[:, 0, 0:1], 0.0).then_inc(prod_free, AHEAD)
            dve.wait_ge(agg_zeroed, 1)
            dve.memset(stats[:, 0, 1:2], 0.0).then_inc(window_ready, 1)
            dve.wait_ge(rows_in, 32)

            def accumulate(g, par, tiles, ahead):
                _, offs = nc.values_load_multi_w_load_instructions(
                    offs_row[0:1, bass.ds(g * 16, 16)], engines=[dve.engine], min_val=0, max_val=P - 1,
                    skip_runtime_bounds_check_because="the offsets are clamped when they are made")
                for j in range(tiles):
                    t = g * TG + j
                    if j == 0:
                        dve.wait_ge(window_ready, g + 1)
                    dve.wait_ge(prod_ready, t + 1)
                    dve.wait_ge(prod_free, t + AHEAD)
                    w = agg[:, par, bass.ds(offs[j], SPAN), :].rearrange("p n r -> p (n r)")
                    dve.tensor_tensor(w, prod[j % AHEAD][:, 0:KEYS], w, ALU.add).then_inc(prod_free, 1)
                    if j + AHEAD < tiles or ahead:
                        make_onehot(t + AHEAD, j % AHEAD)
                return offs[TG]

            def sum_step(g, par):
                nxt = accumulate(g, par, TG, True)
                dve.wait_ge(prod_free, (g + 1) * TG + AHEAD)
                dve.wait_ge(agg_zeroed, g + 2)
                dve.tensor_copy(agg[:, 1 - par, 0, :],
                                agg[:, par, bass.ds(nxt, 1), :].rearrange("p n r -> p (n r)")
                                ).then_inc(window_ready, 1)

            for g in range(EARLY):
                if g + 2 < EARLY:
                    statistics(TABLE_CH + g + 2)
                    scales(TABLE_CH + g + 2)
                sum_step(g, g % 2)
            with dve.Fori(0, CHECK_PAIR) as gg:
                for par in range(2):
                    sum_step(gg * 2 + (EARLY + par), par)

            dve.wait_ge(nxt_in, 48)
            dve.memset(excess[:, :], 0.0).then_inc(dve_step, 1)
            dve.tensor_tensor(key[:, :, :], dst_i[:, :, :], nxt_i[:, :, :], ALU.subtract).then_inc(dve_step, 1)
            steps[0] += 2
            dve.wait_ge(dve_step, steps[0])
            link(dve.tensor_reduce(excess[:, 0:1], key[:, :, :].rearrange("p b e -> p (b e)"), AX.X, ALU.max))
            link(dve.scalar_tensor_tensor(out=key[:, :, :], in0=rel[:, :, :], scalar=PAD / 2,
                                          in1=rel[:, :, :], op0=ALU.is_lt, op1=ALU.mult))
            link(dve.tensor_reduce(excess_max[:, :], key[:, :, :].rearrange("p b e -> p (b e)"), AX.X, ALU.max))
            dve.tensor_scalar(excess[:, 1:2], excess_max[:, :], float(1 - SPAN), None, ALU.add)
            dve.tensor_scalar(excess[0:FULL, 2:3], first_i[0:FULL, TG:TG + 1], first_i[0:FULL, 0:1],
                              float(1 - P), ALU.subtract, ALU.add)
            dve.tensor_scalar(excess[0:FULL, 3:4], first_i[0:FULL, 0:1], float(P - N), None, ALU.add)
            link(dve.tensor_scalar(excess[:, 4:5], last_i[:, :], -1.0, float(N - P), ALU.mult, ALU.add))
            dve.tensor_reduce(excess_max[:, :], excess[:, :], AX.X, ALU.max).then_inc(excess_ready, 1)

            with dve.Fori(CHECK_PAIR, (FULL - EARLY) // 2) as gg:
                for par in range(2):
                    sum_step(gg * 2 + (EARLY + par), par)
            accumulate(FULL, 0, LAST_TILES, False)
            dve.wait_ge(excess_turned, 1)
            link(dve.tensor_reduce(flag_f[0:1, :], flag_bank[0:1, 0:P], AX.X, ALU.max))
            dve.tensor_scalar(flag_i[0:1, :], flag_f[0:1, :], 0.0, None, ALU.is_gt).then_inc(flag_ready, 1)

            with general_path(dve):
                dve.wait_ge(general_x_in, 32)
                dve.tensor_tensor(xh[:, :, :], xh[:, :, :], bias_bc[:, None, :].to_broadcast([P, ROWS, D]),
                                  ALU.add).then_inc(general_biased, 1)
                dve.tensor_tensor(xr[0:REST, :], xr[0:REST, :], bias_bc[0:REST, :], ALU.add
                                  ).then_inc(general_biased, 1)
                dve.wait_ge(general_consts, 1)
                dve.tensor_scalar(before[:, :], places[:, :], part_f[:, :], None, ALU.is_lt
                                  ).then_inc(general_dve, 1)
                dve.wait_ge(general_dve, 1)

                def tile(t, n):
                    done = 6 * t + 1
                    dve.wait_ge(edges_in, 64 * (t + 1))
                    dve.tensor_copy(typ_f[0:n, :], typ_col[0:n, :])
                    dve.tensor_copy(dst_f[0:n, :], dst_col[0:n, :]).then_inc(general_dve, 1)
                    dve.wait_ge(general_dve, done + 1)
                    dve.tensor_scalar(same[0:n, 0:n], dst_row[0:n, 0:n], dst_f[0:n, :], None, ALU.is_equal)
                    dve.tensor_scalar(typ_onehot[0:n, :], keys_iota[0:n, 0, 0:R], typ_f[0:n, :], None, ALU.is_equal
                                      ).then_inc(general_dve, 1)
                    dve.wait_ge(general_dve, done + 2)
                    for r in range(R):
                        last = dve.tensor_scalar(picked[0:n, r, 0:n], same[0:n, 0:n], typ_onehot[0:n, r:r + 1],
                                                 None, ALU.mult)
                    last.then_inc(picked_ready, 1)
                    dve.tensor_tensor(twins[0:n, 0:n], same[0:n, 0:n], before[0:n, 0:n], ALU.mult
                                      ).then_inc(general_dve, 1)
                    dve.wait_ge(general_dve, done + 3)
                    dve.tensor_reduce(twins_f[0:n, :], twins[0:n, 0:n], AX.X, ALU.add).then_inc(general_dve, 1)
                    dve.wait_ge(general_dve, done + 4)
                    dve.tensor_scalar(skip_f[0:n, :], twins_f[0:n, :], 1.0, PAD, ALU.min, ALU.mult
                                      ).then_inc(general_dve, 1)
                    dve.wait_ge(general_dve, done + 5)
                    dve.tensor_tensor(target[0:n, :], skip_f[0:n, :], dst_f[0:n, :], ALU.add
                                      ).then_inc(target_ready, 1)
                    dve.sem_inc(general_dve, 1)
                    dve.wait_ge(rows_scattered, 16 * (t + 1))
                    dve.sem_inc(general_seen, 1)

                general_tiles(dve, tile)

        @block.tensor
        def _(pe):
            pe.wait_ge(consts_set, 1)

            def turn_over(tile, first):
                for k, bs in enumerate(batches()):
                    if first + k >= 2:
                        pe.wait_ge(unturned, first + k - 1)
                    for i, b in enumerate(bs):
                        last = pe.transpose(turn[(first + k) % 2][:, i * P:(i + 1) * P], tile[:, b, :], ident[:, :])
                    last.then_inc(turned, 1)

            pe.wait_ge(srcf_ready, 1)
            turn_over(key, 0)
            pe.wait_ge(key_ready, 1)
            turn_over(key, len(batches()))
            pe.wait_ge(w_in, 32 * Q)
            for k in range(W_BANKS):
                if w_banks[k] in turn:
                    pe.wait_ge(unturned, 2 * len(batches()))
                n = DQ // W_BANKS
                for o in range(n):
                    last = pe.matmul(w_banks[k][:, o * Q * R:(o + 1) * Q * R], wt[:, :, k * n + o],
                                     wc_q[:, :, :].rearrange("p q r -> p (q r)"), start=True, stop=True)
                last.then_inc(w_turned, 1)
            pe.wait_ge(bias_in, 16)

            def mix_parts(g, par, tiles, rows, rows_done, rows_count):
                def x_part():
                    pe.wait_ge(rows_done, rows_count)
                    pe.matmul(mix[par][:, 0:D], ident[:, :], rows, start=True, stop=False)

                def bias_part():
                    pe.matmul(mix[par][:, 0:D], ident[:, :], bias_bc[:, :], start=False, stop=False)

                def relation(r):
                    if r == 0:
                        pe.wait_ge(prod_free, g * TG + tiles + AHEAD)
                    last = pe.matmul(mix[par][:, 0:D], agg[:, par, 0:P, r], W[:, r, :],
                                     start=False, stop=(r == R - 1))
                    if r == R - 1:
                        last.then_inc(mixed, 1)

                return [x_part, bias_part] + [lambda r=r: relation(r) for r in range(R)]

            def products(g, tiles, early=False, parts=()):
                each = -(-len(parts) // MIX_TILES)
                for j in range(tiles):
                    t = g * TG + j
                    if not early:
                        pe.wait_ge(gathered[j], (g - EARLY + 1) * 16)
                    elif j == 0:
                        pe.wait_ge(h_ready, turn_of[TABLE_CH + g] + 1)
                    sources = G_early[:, g, j, :] if early else G[:, j, :]
                    pe.wait_ge(onehot_ready, t + 1)
                    pe.wait_ge(prod_free, t + 1)
                    pe.matmul(prod[j % AHEAD][:, 0:KEYS], sources, onehot[:, j % AHEAD, :],
                              start=True, stop=True).then_inc(prod_ready, 1)
                    for part in parts[j * each:(j + 1) * each]:
                        part()

            def early_mix(g):
                return mix_parts(g, g % 2, TG, x_t[:, g % 2, :], xt_in[g % 2], (g // 2 + 1) * 16)

            products(0, TG, early=True)
            pe.wait_ge(w_ready, W_BANKS)
            for g in range(1, EARLY):
                products(g, TG, early=True, parts=early_mix(g - 1))
            for part in early_mix(EARLY - 1):
                part()
            with pe.Fori(0, (FULL - EARLY) // 2) as gg:
                for par in range(2):
                    g = gg * 2 + (EARLY + par)
                    products(g, TG)
                    for part in mix_parts(g, par, TG, x_t[:, par, :], xt_in[par], gg * 16 + (EARLY // 2 + 1) * 16):
                        part()
            pe.wait_ge(excess_ready, 1)
            pe.transpose(flag_bank[0:1, 0:P], excess_max[:, :], ident[:, :]).then_inc(excess_turned, 1)
            products(FULL, LAST_TILES)
            for part in mix_parts(FULL, 0, LAST_TILES, x_last[:, :], x_last_in, 16):
                part()

            with general_path(pe):
                def tile(t, n):
                    pe.wait_ge(picked_ready, t + 1)
                    pe.wait_ge(rows_gathered, 32 * (t + 1))
                    for k in range(R // 4):
                        last = pe.matmul(sum_banks[k][:, :].rearrange("p (r e) -> p r e", e=P)[:, :, 0:n],
                                         h_rows[0:n, :], picked[0:n, 4 * k:4 * k + 4, 0:n], start=True, stop=True)
                    last.then_inc(sums_ready, 1)
                    pe.matmul(mix[0][0:n, 0:D], ident[0:n, 0:n], out_rows[0:n, :], start=True, stop=False)
                    pe.wait_ge(sums_moved, t + 1)
                    for r in range(R):
                        last = pe.matmul(mix[0][0:n, 0:D], sums[:, r, 0:n], W[:, r, :],
                                         start=False, stop=(r == R - 1))
                    last.then_inc(new_rows_ready, 1)

                general_tiles(pe, tile)


_INS = ['x', 'src', 'dst', 'edge_type_16', 'L0_gnn_weight', 'L0_gnn_w_comp', 'L0_gnn_h_bias']


def kernel(**inputs):
    import numpy as _np
    import concourse.bacc as _bacc
    from concourse import mybir as _mybir
    from concourse.bass_utils import run_bass_kernel_spmd as _run

    nc = _bacc.Bacc("TRN2", target_bir_lowering=False, num_devices=1)
    arrays, args = {}, []
    for name in _INS:
        a = _np.ascontiguousarray(inputs[name])
        arrays[f"in_{name}_dram"] = a
        args.append(nc.dram_tensor(f"in_{name}_dram", a.shape, _mybir.dt.from_np(a.dtype), kind="ExternalInput").ap())
    out = nc.dram_tensor("out_0_dram", inputs["x"].shape, _mybir.dt.float32, kind="ExternalOutput").ap()
    gnn_kernel(nc, *args, out)
    return _run(nc, [arrays], core_ids=[0]).results[0]["out_0_dram"]
```

```python
import concourse.bass as bass
from concourse import mybir
from contextlib import ExitStack



def gnn_kernel(nc, x, src, dst, etype, weight, w_comp, h_bias, out):
    F32 = mybir.dt.float32
    I32 = mybir.dt.int32
    ALU = mybir.AluOpType
    ACT = mybir.ActivationFunctionType
    AX = mybir.AxisListType

    P = 128
    N, D = x.shape
    E = src.shape[0]
    B = weight.shape[0]
    R = w_comp.shape[0]
    EPS = 1e-5
    DVE_ROWS = 3

    TILES = -(-E // P)
    BLOCKS = -(-TILES // P)
    TG = 15
    GROUPS = -(-TILES // TG)
    LAST_TILES = TILES - (GROUPS - 1) * TG
    FULL = GROUPS - 1
    SPAN = 13
    KEYS = SPAN * R
    WIN = P + SPAN
    EARLY_GROUPS = 21
    EARLY_TILES = 3
    TABLE_TILES = TG - EARLY_TILES
    EARLY = EARLY_GROUPS * EARLY_TILES
    EARLY_CH = 9
    assert FULL % 2 == 0 and EARLY_GROUPS % 2 == 1 and EARLY % EARLY_CH == 0
    RUNS = ((1, EARLY_GROUPS - 1, True), (EARLY_GROUPS, FULL - 1 - EARLY_GROUPS, False))
    MIX_FROM = 2
    MIX_EACH = 2
    AHEAD = 3
    IDX_A = 8
    W_BANKS = R * D // 512
    CHECK_PAIR = 20
    Q = 4
    DQ = D // Q
    PAD = float(1 << 20)

    ROWS = N // P
    MAIN = ROWS * P
    REST = N - MAIN
    CH = 16
    CHUNKS = [(c, min(c + CH, ROWS)) for c in range(0, ROWS - ROWS % CH, CH)]
    if ROWS % CH:
        if ROWS % CH < 4:
            CHUNKS[-1] = (CHUNKS[-1][0], ROWS)
        else:
            CHUNKS.append((ROWS - ROWS % CH, ROWS))
    TABLE_CH = len(CHUNKS) + 1
    NORM_CH = TABLE_CH + EARLY // EARLY_CH
    STAT_ROWS = ROWS + 1 + EARLY

    FB = (BLOCKS - 1) * P * P
    TAIL_T = (E - FB) // P
    TAIL_E = E - FB - TAIL_T * P

    h_dram = nc.dram_tensor("h_table", (N, D), F32).ap()
    offs_dram = nc.dram_tensor("offs_scratch", (GROUPS, 16), I32).ap()
    base_dram = nc.dram_tensor("base_scratch", (GROUPS, 1), I32).ap()

    with ExitStack() as ctx:
        def sb(name, shape, dt=F32):
            return ctx.enter_context(nc.sbuf_tensor(name, shape, dt))

        def sem(name):
            return ctx.enter_context(nc.semaphore(name))

        xh = sb("xh", [P, ROWS, D])
        xr = sb("xr", [P, D])
        stats = sb("stats", [P, STAT_ROWS, 6])
        mean2 = sb("mean2", [P, STAT_ROWS])
        mdiff = sb("mdiff", [P, STAT_ROWS])
        var = sb("var", [P, STAT_ROWS])
        std = sb("std", [P, STAT_ROWS])
        rstd = sb("rstd", [P, STAT_ROWS])
        shift = sb("shift", [P, STAT_ROWS])
        eps_c = sb("eps_c", [P, 1])

        src_i = sb("src_i", [P, BLOCKS, P], I32)
        dst_i = sb("dst_i", [P, BLOCKS, P], I32)
        nxt_i = sb("nxt_i", [P, BLOCKS, P], I32)
        typ_i = sb("typ_i", [P, BLOCKS, P], I32)
        rel = sb("rel", [P, BLOCKS, P])
        key = sb("key", [P, BLOCKS, P])
        src_t = sb("src_t", [P, BLOCKS * P + TG], I32)
        key_t = sb("key_t", [P, BLOCKS * P])

        first_i = sb("first_i", [GROUPS, 16], I32)
        offs_f = sb("offs_f", [GROUPS, 16])
        offs_i = sb("offs_i", [GROUPS, 16], I32)
        base_i = sb("base_i", [GROUPS, 1], I32)
        offs_row = sb("offs_row", [1, GROUPS * 16], I32)
        base_row = sb("base_row", [1, GROUPS], I32)
        last_i = sb("last_i", [P, 1], I32)
        part_f = sb("part_f", [P, 1])
        last_idx = sb("last_idx", [P, 1], I32)
        ident = sb("ident", [P, P])
        keys_iota = sb("keys_iota", [P, SPAN, R + 1])
        zeros = sb("zeros", [P, R])

        wt = sb("wt", [Q * B, D, DQ])
        wc_q = sb("wc_q", [Q * B, Q, R])
        W = sb("W", [P, R, D])
        bias_bc = sb("bias_bc", [P, D])

        idx = sb("idx", [P, TG], I32)
        G = sb("G", [P, TG, D])
        X_early = sb("X_early", [P, EARLY, D])
        onehot = sb("onehot", [P, AHEAD, KEYS])
        agg = sb("agg", [P, 2, WIN, R])
        x_t = sb("x_t", [P, 2, D])
        x_last = sb("x_last", [P, D])
        out_sb = sb("out_sb", [P, 2, D])

        excess = sb("excess", [P, 5])
        excess_max = sb("excess_max", [P, 1])
        flag_f = sb("flag_f", [1, 1])
        flag_i = sb("flag_i", [1, 1], I32)

        picked = xh[:, 0:R, :]
        sums = xh[:, R:2 * R, :]
        same = xh[:, 2 * R, :]
        before = xh[:, 2 * R + 1, :]
        twins = xh[:, 2 * R + 2, :]
        h_rows = xh[:, 2 * R + 3, :]
        out_rows = xh[:, 2 * R + 4, :]
        new_rows = xh[:, 2 * R + 5, :]
        places = xh[:, 2 * R + 6, :]
        typ_onehot = xh[:, 2 * R + 7, 0:R]
        dst_f = xh[:, 2 * R + 8, 0:1]
        typ_f = xh[:, 2 * R + 8, 1:2]
        twins_f = xh[:, 2 * R + 8, 2:3]
        skip_f = xh[:, 2 * R + 8, 3:4]
        dst_row = dst_i[:, 0, :]
        dst_col = typ_i[:, 0, 0:1]
        src_col = typ_i[:, 0, 1:2]
        typ_col = typ_i[:, 0, 2:3]
        target = typ_i[:, 0, 3:4]

        def bank(name):
            return ctx.enter_context(nc.psum_tensor(name, [P, 512], F32))

        prod = [bank(f"prod{i}") for i in range(AHEAD)]
        mix = [bank(f"mix{i}") for i in range(2)]
        flag_bank = bank("flag_bank")
        sum_banks = prod + [flag_bank]
        turn = [bank(f"turn{i}") for i in range(2)]
        w_banks = mix + turn

        x_in = [sem(f"x_in{i}") for i in range(TABLE_CH)]
        src_first_in = sem("src_first_in")
        src_in = sem("src_in")
        dst_in = sem("dst_in")
        typ_in = sem("typ_in")
        first_in = sem("first_in")
        w_in = sem("w_in")
        bias_in = sem("bias_in")
        pads_set = sem("pads_set")
        consts_set = sem("consts_set")
        dve_step = sem("dve_step")
        pool_step = sem("pool_step")
        var_ready = sem("var_ready")
        std_ready = sem("std_ready")
        norm_ready = sem("norm_ready")
        h_ready = sem("h_ready")
        h_dve_ready = sem("h_dve_ready")
        h_stored = sem("h_stored")
        offs_ready = sem("offs_ready")
        offs_stored = sem("offs_stored")
        rows_in = sem("rows_in")
        key_ready = sem("key_ready")
        srcf_ready = sem("srcf_ready")
        turned = sem("turned")
        unturned = sem("unturned")
        w_turned = sem("w_turned")
        w_ready = sem("w_ready")
        idx_seen = sem("idx_seen")
        window_ready = sem("window_ready")
        out_free = sem("out_free")
        x_last_in = sem("x_last_in")
        idx_ready = [sem("idx_ready_a"), sem("idx_ready_b")]
        early_in = [sem(f"early_in{c}") for c in range(EARLY // EARLY_CH)]
        early_placed = sem("early_placed")
        gathered = [sem(f"gathered{j}") for j in range(TG)]
        onehot_ready = sem("onehot_ready")
        prod_ready = sem("prod_ready")
        prod_free = sem("prod_free")
        agg_zeroed = sem("agg_zeroed")
        xt_in = [sem("xt_in0"), sem("xt_in1")]
        mixed = sem("mixed")
        out_ready = sem("out_ready")
        out_stored = sem("out_stored")
        last_in = sem("last_in")
        nxt_in = sem("nxt_in")
        last_idx_ready = sem("last_idx_ready")
        last_stored = sem("last_stored")
        excess_ready = sem("excess_ready")
        excess_turned = sem("excess_turned")
        flag_ready = sem("flag_ready")
        general_x_in = sem("general_x_in")
        general_dve = sem("general_dve")
        general_biased = sem("general_biased")
        general_based = sem("general_based")
        general_consts = sem("general_consts")
        general_seen = sem("general_seen")
        edges_in = [sem(f"edges_in_{a}") for a in ("dst", "src", "typ", "dst_row")]
        rows_gathered = [sem(f"rows_gathered_{a}") for a in ("h", "out")]
        picked_ready = sem("picked_ready")
        target_ready = sem("target_ready")
        sums_ready = sem("sums_ready")
        sums_moved = sem("sums_moved")
        new_rows_ready = sem("new_rows_ready")
        new_rows_moved = sem("new_rows_moved")
        rows_scattered = sem("rows_scattered")

        block = ctx.enter_context(nc.Block())

        def edge_loads(eng, a, tile, done, skip=0, block=0):
            a = a[skip:E] if skip else a
            eng.dma_start(tile[:, block:BLOCKS - 1, :],
                          a[block * P * P:FB].rearrange("(b p e) -> p b e", p=P, e=P)).then_inc(done, 16)
            eng.dma_start(tile[0:TAIL_T, BLOCKS - 1, :],
                          a[FB:FB + TAIL_T * P].rearrange("(p e) -> p e", e=P)).then_inc(done, 16)
            eng.dma_start(tile[TAIL_T:TAIL_T + 1, BLOCKS - 1, 0:TAIL_E - skip],
                          a[FB + TAIL_T * P:E - skip].rearrange("(p e) -> p e", p=1)).then_inc(done, 16)

        def x_chunk(c):
            if c == TABLE_CH - 1:
                return xr[0:REST, :], x[MAIN:N, :], h_dram[MAIN:N, :]
            a, b = CHUNKS[c]
            xv = x[0:MAIN, :].rearrange("(p r) d -> p r d", p=P)
            hv = h_dram[0:MAIN, :].rearrange("(p r) d -> p r d", p=P)
            return xh[:, a:b, :], xv[:, a:b, :], hv[:, a:b, :]

        def norm_chunk(c):
            if c >= TABLE_CH:
                k = c - TABLE_CH
                a = ROWS + 1 + k * EARLY_CH
                return P, a, a + EARLY_CH, lambda r: X_early[:, r - ROWS - 1, :], early_in[k], 16 * EARLY_CH
            if c == TABLE_CH - 1:
                return REST, ROWS, ROWS + 1, lambda r: xr[0:REST, :], x_in[c], 16
            a, b = CHUNKS[c]
            return P, a, b, lambda r: xh[:, r, :], x_in[c], 16

        def dve_rows(c):
            return DVE_ROWS if c < TABLE_CH - 1 else 0

        def batches():
            return [list(range(b, min(b + 4, BLOCKS))) for b in range(0, BLOCKS, 4)]

        def general_path(eng):
            eng.wait_ge(flag_ready, 1)
            return eng.If(eng.value_load(flag_i[0:1, 0:1], min_val=0, max_val=1) > 0)

        def general_tiles(eng, tile):
            with eng.Fori(0, TILES - 1) as t:
                tile(t, P)
            tile(TILES - 1, TAIL_E)

        @block.sync
        def _(sp):
            sp.dma_start(src_i[:, 0:4, :], src[0:4 * P * P].rearrange("(b p e) -> p b e", p=P, e=P)
                         ).then_inc(src_first_in, 16)
            sp.wait_ge(pads_set, 6)
            edge_loads(sp, src, src_i, src_in, block=4)
            edge_loads(sp, dst, dst_i, dst_in)
            edge_loads(sp, etype, typ_i, typ_in)
            sp.dma_start(first_i[0:FULL, 0:TG], dst[0:FULL * TG * P].rearrange(
                "(g i e) -> g i e", i=TG, e=P)[:, :, 0], allow_slow_non_contiguous=True).then_inc(first_in, 16)
            sp.dma_start(first_i[0:FULL, TG:TG + 1], dst[TG * P:TG * P * FULL + 1:TG * P].rearrange(
                "(g i) -> g i", i=1), allow_slow_non_contiguous=True).then_inc(first_in, 16)
            sp.dma_start(first_i[FULL:GROUPS, 0:LAST_TILES], dst[FULL * TG * P:E:P].rearrange(
                "(g i) -> g i", g=1), allow_slow_non_contiguous=True).then_inc(first_in, 16)
            sp.dma_start(last_i[:, :], dst[FULL * TG * P:FULL * TG * P + 1].partition_broadcast(P)
                          ).then_inc(last_in, 16)
            for c in range(TABLE_CH):
                dstn, srcn, _ = x_chunk(c)
                sp.dma_start(dstn, srcn).then_inc(x_in[c], 16)
            for q in range(Q):
                rows = slice(q * B, (q + 1) * B)
                sp.dma_start(wt[rows, :, :], weight[:, :, q * DQ:(q + 1) * DQ]).then_inc(w_in, 16)
                sp.dma_start(wc_q[rows, q, :], w_comp.rearrange("r b -> b r"), allow_slow_non_contiguous=True
                              ).then_inc(w_in, 16)
            sp.dma_start(bias_bc[:, :], h_bias.partition_broadcast(P)).then_inc(bias_in, 16)
            sp.sem_inc(out_free, 2)
            sp.wait_ge(offs_ready, 2)
            sp.dma_start(offs_dram[:, :], offs_i[:, :]).then_inc(offs_stored, 16)
            sp.dma_start(base_dram[:, :], base_i[:, :]).then_inc(offs_stored, 16)
            sp.wait_ge(offs_stored, 32)
            sp.dma_start(offs_row[:, :], offs_dram.rearrange("(a g) i -> a (g i)", a=1)).then_inc(rows_in, 16)
            sp.dma_start(base_row[:, :], base_dram.rearrange("(a g) i -> a (g i)", a=1)).then_inc(rows_in, 16)
            for c in range(TABLE_CH):
                srcn, _, dstn = x_chunk(c)
                if dve_rows(c):
                    sp.wait_ge(h_dve_ready, c + 1)
                sp.wait_ge(h_ready, c + 1)
                sp.dma_start(dstn, srcn).then_inc(h_stored, 16)
            edge_loads(sp, dst, nxt_i, nxt_in, skip=1)
            sp.wait_ge(rows_in, 32)
            with sp.Fori(0, FULL // 2) as gg:
                for par in range(2):
                    g = gg * 2 + par
                    base = sp.value_load(base_row[0:1, bass.ds(g, 1)], min_val=0, max_val=N - P)
                    sp.dma_start(x_t[:, par, :], x[bass.ds(base, P), :]).then_inc(xt_in[par], 16)
                    sp.wait_ge(out_ready, g + 1)
                    sp.dma_start(out[bass.ds(base, P), :], out_sb[:, par, :]).then_inc(out_stored, 16)
                    sp.wait_ge(out_stored, (g + 1) * 16)
                    sp.sem_inc(out_free, 1)

            with general_path(sp):
                sp.wait_ge(h_stored, 16 * TABLE_CH)
                sp.wait_ge(last_stored, 16)
                sp.dma_start(xh[:, :, :], x[0:MAIN, :].rearrange("(p r) d -> p r d", p=P)).then_inc(general_x_in, 16)
                sp.dma_start(xr[0:REST, :], x[MAIN:N, :]).then_inc(general_x_in, 16)
                sp.wait_ge(general_biased, 2)
                sp.dma_start(out[0:MAIN, :].rearrange("(p r) d -> p r d", p=P), xh[:, :, :]).then_inc(general_based, 16)
                sp.dma_start(out[MAIN:N, :], xr[0:REST, :]).then_inc(general_based, 16)
                sp.wait_ge(general_based, 32)

                def tile(t, n):
                    edges = bass.ds(t * P, n)
                    for k, (col, a) in enumerate(((dst_col, dst), (src_col, src), (typ_col, etype))):
                        sp.dma_start(col[0:n, :], a[edges].rearrange("(p o) -> p o", o=1),
                                     allow_slow_non_contiguous=True).then_inc(edges_in[k], 16)
                    sp.dma_start(dst_row[0:n, 0:n], dst[edges].partition_broadcast(n)).then_inc(edges_in[3], 16)
                    sp.wait_ge(rows_scattered, 16 * (t + 1))
                    sp.sem_inc(general_seen, 1)

                general_tiles(sp, tile)

        @block.gpsimd
        def _(pool):
            pool.memset(src_i[:, BLOCKS - 1, :], 0).then_inc(pads_set, 1)
            pool.memset(dst_i[:, BLOCKS - 1, :], int(PAD)).then_inc(pads_set, 1)
            pool.memset(nxt_i[:, BLOCKS - 1, :], int(PAD)).then_inc(pads_set, 1)
            pool.memset(typ_i[:, BLOCKS - 1, :], 0).then_inc(pads_set, 1)
            pool.memset(first_i[:, :], int(PAD)).then_inc(pads_set, 1)
            pool.memset(wc_q[:, :, :], 0.0).then_inc(pads_set, 1)
            pool.memset(ident[:, :], 0.0).then_inc(pool_step, 1)
            pool.wait_ge(pool_step, 1)
            pool.affine_select(out=ident[:, :], in_=ident[:, :], compare_op=ALU.not_equal, fill=1.0,
                               base=0, pattern=[[-1, P]], channel_multiplier=1).then_inc(consts_set, 1)
            pool.iota(keys_iota[:, :, :], pattern=[[R, SPAN], [1, R + 1]], base=0, channel_multiplier=0,
                      allow_small_or_imprecise_dtypes=True).then_inc(consts_set, 1)
            pool.iota(part_f[:, :], pattern=[[0, 1]], base=0, channel_multiplier=1,
                      allow_small_or_imprecise_dtypes=True).then_inc(consts_set, 1)
            pool.memset(zeros[:, :], 0.0).then_inc(consts_set, 1)
            pool.memset(eps_c[:, :], EPS).then_inc(consts_set, 1)
            pool.memset(src_t[:, BLOCKS * P:], 0).then_inc(consts_set, 1)
            pool.memset(x_last[:, :], 0.0).then_inc(pool_step, 1)
            pool.wait_ge(unturned, 1)
            for e in range(EARLY):
                t = e // EARLY_TILES * TG + TABLE_TILES + e % EARLY_TILES
                pool.indirect_dma_start(X_early[:, e, :], None, x[:, :],
                                        bass.IndirectOffsetOnAxis(ap=src_t[:, t:t + 1], axis=0)
                                        ).then_inc(early_in[e // EARLY_CH], 16)
            pool.wait_ge(last_idx_ready, 2)
            pool.wait_ge(pool_step, 2)
            pool.indirect_dma_start(x_last[:, :], None, x[:, :],
                                    bass.IndirectOffsetOnAxis(ap=last_idx[:, 0:1], axis=0),
                                    bounds_check=N - 1, oob_is_err=False).then_inc(x_last_in, 16)

            pool.wait_ge(h_stored, 16 * TABLE_CH)

            def gathers(g, tiles):
                for j in range(tiles):
                    if j == 0:
                        pool.wait_ge(idx_ready[0], g + 1)
                        pool.sem_inc(idx_seen, 1)
                    if j == IDX_A:
                        pool.wait_ge(idx_ready[1], g + 1)
                        pool.sem_inc(idx_seen, 1)
                    pool.indirect_dma_start(G[:, j, :], None, h_dram[:, :],
                                            bass.IndirectOffsetOnAxis(ap=idx[:, j:j + 1], axis=0)
                                            ).then_inc(gathered[j], 16)

            with pool.Fori(0, EARLY_GROUPS) as g:
                gathers(g, TABLE_TILES)
            with pool.Fori(EARLY_GROUPS, FULL) as g:
                gathers(g, TG)
            gathers(FULL, LAST_TILES)
            pool.wait_ge(out_ready, GROUPS)
            pool.wait_ge(out_stored, 16 * FULL)
            pool.indirect_dma_start(out[:, :], bass.IndirectOffsetOnAxis(ap=last_idx[:, 0:1], axis=0),
                                    out_sb[:, 0, :], None, bounds_check=N - 1,
                                    oob_is_err=False).then_inc(last_stored, 16)
            pool.wait_ge(last_stored, 16)

            with general_path(pool):
                pool.wait_ge(general_based, 32)
                pool.iota(places[:, :], pattern=[[1, P]], base=0, channel_multiplier=0,
                          allow_small_or_imprecise_dtypes=True).then_inc(general_consts, 1)

                def tile(t, n):
                    pool.wait_ge(edges_in[0], 16 * (t + 1))
                    pool.wait_ge(edges_in[1], 16 * (t + 1))
                    pool.sem_inc(general_seen, 1)
                    pool.indirect_dma_start(h_rows[0:n, :], None, h_dram[:, :],
                                            bass.IndirectOffsetOnAxis(ap=src_col[0:n, :], axis=0)
                                            ).then_inc(rows_gathered[0], 16)
                    pool.indirect_dma_start(out_rows[0:n, :], None, out[:, :],
                                            bass.IndirectOffsetOnAxis(ap=dst_col[0:n, :], axis=0)
                                            ).then_inc(rows_gathered[1], 16)
                    pool.wait_ge(new_rows_moved, t + 1)
                    pool.wait_ge(target_ready, t + 1)
                    pool.sem_inc(general_seen, 1)
                    pool.indirect_dma_start(out[:, :], bass.IndirectOffsetOnAxis(ap=target[0:n, :], axis=0),
                                            new_rows[0:n, :], None, bounds_check=N - 1,
                                            oob_is_err=False).then_inc(rows_scattered, 16)

                general_tiles(pool, tile)
                pool.wait_ge(rows_scattered, 16 * TILES)

        @block.scalar
        def _(act):
            act.wait_ge(src_first_in, 16)
            act.activation(key[:, 0:4, :], src_i[:, 0:4, :], ACT.Copy).then_inc(srcf_ready, 1)
            for k, bs in enumerate(batches()):
                if k == 1:
                    act.wait_ge(src_in, 48)
                    act.activation(key[:, 4:BLOCKS, :], src_i[:, 4:BLOCKS, :], ACT.Copy).then_inc(srcf_ready, 1)
                act.wait_ge(turned, k + 1)
                act.activation(src_t[:, bs[0] * P:(bs[-1] + 1) * P], turn[k % 2][:, 0:len(bs) * P],
                               ACT.Copy).then_inc(unturned, 1)
            act.wait_ge(unturned, len(batches()))
            act.wait_ge(consts_set, 6)
            for half, (a, b) in enumerate(((0, IDX_A), (IDX_A, TG))):
                act.activation(idx[:, a:b], src_t[:, a:b], ACT.Copy
                               ).then_inc(idx_ready[half], 1)
            for par in range(2):
                act.activation(agg[:, par, :, :], zeros[:, None, :].to_broadcast([P, WIN, R]),
                               ACT.Copy).then_inc(agg_zeroed, 1)

            for k, bs in enumerate(batches()):
                act.wait_ge(turned, len(batches()) + k + 1)
                act.activation(key_t[:, bs[0] * P:(bs[-1] + 1) * P],
                               turn[(k + len(batches())) % 2][:, 0:len(bs) * P], ACT.Copy).then_inc(unturned, 1)

            def place_w(k):
                n = DQ // W_BANKS
                act.wait_ge(w_turned, k + 1)
                act.activation(W[:, :, :].rearrange("p r (q o) -> p o q r", q=Q)[:, k * n:(k + 1) * n, :, :],
                               w_banks[k][:, :].rearrange("p (o q r) -> p o q r", q=Q, r=R),
                               ACT.Copy).then_inc(w_ready, 1)

            def root(c):
                parts, a, b = norm_chunk(c)[:3]
                act.wait_ge(var_ready, c + 1)
                act.activation(std[0:parts, a:b], var[0:parts, a:b], ACT.Sqrt,
                               bias=eps_c[0:parts, :]).then_inc(std_ready, 1)

            def relus(c):
                parts, a, b, row = norm_chunk(c)[:4]
                act.wait_ge(norm_ready, c + 1)
                for r in range(a, b - dve_rows(c)):
                    last = act.activation(row(r), row(r), ACT.Relu, bias=shift[0:parts, r:r + 1],
                                          scale=rstd[0:parts, r:r + 1])
                last.then_inc(h_ready, 1)

            root(0)
            for c in range(TABLE_CH):
                if c + 1 < TABLE_CH:
                    root(c + 1)
                relus(c)
            for k in range(W_BANKS):
                place_w(k)
            for c in range(TABLE_CH, NORM_CH):
                root(c)
            act.wait_ge(norm_ready, NORM_CH)

            def evacuate(g, par):
                act.wait_ge(mixed, g + 1)
                act.wait_ge(out_free, g + 1)
                act.activation(out_sb[:, par, :], mix[par][:, 0:D], ACT.Copy).then_inc(out_ready, 1)

            def renew(g, par):
                act.wait_ge(window_ready, g + 2)
                act.activation(agg[:, par, :, :], zeros[:, None, :].to_broadcast([P, WIN, R]),
                               ACT.Copy).then_inc(agg_zeroed, 1)

            def step(g, par, early, first=False):
                if early:
                    for i in range(EARLY_TILES):
                        e = g * EARLY_TILES + i
                        col = bass.ds(e + (ROWS + 1), 1)
                        last = act.activation(G[:, TABLE_TILES + i, :],
                                              X_early[:, bass.ds(e, 1), :].rearrange("p e d -> p (e d)"),
                                              ACT.Relu, bias=shift[:, col], scale=rstd[:, col])
                    last.then_inc(early_placed, 1)
                for half, (a, b) in enumerate(((0, IDX_A), (IDX_A, TG))):
                    act.wait_ge(prod_ready, g * TG + b)
                    act.activation(idx[:, a:b], src_t[:, bass.ds((g + 1) * TG + a, b - a)],
                                   ACT.Copy).then_inc(idx_ready[half], 1)
                    if half == 0 and not first:
                        evacuate(g - 1, 1 - par)
                        renew(g - 1, 1 - par)

            step(0, 0, True, first=True)
            for start, groups, early in RUNS:
                with act.Fori(0, groups // 2) as gg:
                    for i in range(2):
                        step(gg * 2 + (start + i), (start + i) % 2, early)
            step(FULL - 1, 1, False)
            evacuate(FULL - 1, 1)
            evacuate(FULL, 0)

            with general_path(act):
                def tile(t, n):
                    act.wait_ge(sums_ready, t + 1)
                    for k in range(R // 4):
                        last = act.activation(sums[:, 4 * k:4 * k + 4, 0:n],
                                              sum_banks[k][:, :].rearrange("p (r e) -> p r e", e=P)[:, :, 0:n],
                                              ACT.Copy)
                    last.then_inc(sums_moved, 1)
                    act.wait_ge(new_rows_ready, t + 1)
                    act.activation(new_rows[0:n, :], mix[0][0:n, 0:D], ACT.Copy).then_inc(new_rows_moved, 1)

                general_tiles(act, tile)

        @block.vector
        def _(dve):
            steps = [0]

            def link(instruction):
                steps[0] += 1
                instruction.then_inc(dve_step, 1)
                dve.wait_ge(dve_step, steps[0])

            def statistics(c):
                parts, a, b, row, done, count = norm_chunk(c)
                dve.wait_ge(done, count)
                for r in range(a, b):
                    last = dve.bn_stats(stats[0:parts, r, :], row(r))
                link(last)
                s = stats[0:parts, a:b, :]
                m = slice(a, b)
                dve.tensor_tensor(mean2[0:parts, m], s[:, :, 1], s[:, :, 4], ALU.add)
                dve.tensor_tensor(var[0:parts, m], s[:, :, 2], s[:, :, 5], ALU.add)
                link(dve.tensor_tensor(mdiff[0:parts, m], s[:, :, 1], s[:, :, 4], ALU.subtract))
                link(dve.scalar_tensor_tensor(out=mdiff[0:parts, m], in0=mdiff[0:parts, m], scalar=0.25,
                                              in1=mdiff[0:parts, m], op0=ALU.mult, op1=ALU.mult))
                dve.scalar_tensor_tensor(out=var[0:parts, m], in0=var[0:parts, m], scalar=1.0 / D,
                                         in1=mdiff[0:parts, m], op0=ALU.mult, op1=ALU.add
                                         ).then_inc(var_ready, 1)

            def scales(c):
                parts, a, b, row = norm_chunk(c)[:4]
                dve.wait_ge(std_ready, c + 1)
                link(dve.reciprocal(rstd[0:parts, a:b], std[0:parts, a:b]))
                dve.scalar_tensor_tensor(out=shift[0:parts, a:b], in0=mean2[0:parts, a:b], scalar=-0.5,
                                         in1=rstd[0:parts, a:b], op0=ALU.mult, op1=ALU.mult
                                         ).then_inc(norm_ready, 1)
                if dve_rows(c):
                    dve.wait_ge(norm_ready, c + 1)
                    for r in range(b - dve_rows(c), b):
                        last = dve.tensor_scalar(row(r), row(r), rstd[0:parts, r:r + 1], shift[0:parts, r:r + 1],
                                                 ALU.mult, ALU.add)
                    link(last)
                    rows = xh[:, b - dve_rows(c):b, :]
                    dve.tensor_scalar(rows, rows, 0.0, None, ALU.max).then_inc(h_dve_ready, 1)

            dve.wait_ge(dst_in, 48)
            link(dve.tensor_tensor(rel[:, :, :], dst_i[:, :, :], dst_i[:, :, 0:1].to_broadcast([P, BLOCKS, P]),
                                   ALU.subtract))
            dve.wait_ge(typ_in, 48)
            dve.wait_ge(turned, len(batches()))
            dve.scalar_tensor_tensor(out=key[:, :, :], in0=rel[:, :, :], scalar=float(R), in1=typ_i[:, :, :],
                                     op0=ALU.mult, op1=ALU.add).then_inc(key_ready, 1)

            dve.wait_ge(last_in, 16)
            dve.wait_ge(consts_set, 6)
            dve.tensor_tensor(last_idx[:, :], last_i[:, :], part_f[:, :], ALU.add).then_inc(last_idx_ready, 2)
            dve.wait_ge(first_in, 48)
            link(dve.memset(first_i[0:1, 0:1], 0))
            link(dve.tensor_scalar(offs_f[:, :], first_i[:, :], first_i[:, 0:1], float(P - 1),
                                   ALU.subtract, ALU.min))
            dve.tensor_scalar(offs_i[:, :], offs_f[:, :], 0.0, None, ALU.max).then_inc(offs_ready, 1)
            dve.tensor_scalar(base_i[:, :], first_i[:, 0:1], float(N - P), None, ALU.min).then_inc(offs_ready, 1)

            def check_spans():
                dve.wait_ge(unturned, 2 * len(batches()))
                link(dve.memset(excess[:, :], 0.0))
                link(dve.scalar_tensor_tensor(out=key[:, :, :], in0=rel[:, :, :], scalar=PAD / 2,
                                              in1=rel[:, :, :], op0=ALU.is_lt, op1=ALU.mult))
                link(dve.tensor_reduce(excess_max[:, :], key[:, :, :].rearrange("p b e -> p (b e)"), AX.X, ALU.max))
                dve.tensor_scalar(excess[:, 1:2], excess_max[:, :], float(1 - SPAN), None, ALU.add)

            for c in range(NORM_CH):
                statistics(c)
                if c:
                    scales(c - 1)
                if c == NORM_CH - 2:
                    check_spans()
            scales(NORM_CH - 1)

            def make_onehot(t, slot):
                dve.tensor_scalar(onehot[:, slot, :], keys_iota[:, :, 0:R], key_t[:, bass.ds(t, 1)], None,
                                  ALU.is_equal).then_inc(onehot_ready, 1)

            dve.wait_ge(unturned, 2 * len(batches()))
            for t in range(AHEAD):
                make_onehot(t, t)
            dve.memset(stats[:, 0, 0:1], 0.0).then_inc(prod_free, AHEAD)
            dve.wait_ge(agg_zeroed, 1)
            dve.memset(stats[:, 0, 1:2], 0.0).then_inc(window_ready, 1)
            dve.wait_ge(rows_in, 32)

            def accumulate(g, par, tiles, ahead):
                _, offs = nc.values_load_multi_w_load_instructions(
                    offs_row[0:1, bass.ds(g * 16, 16)], engines=[dve.engine], min_val=0, max_val=P - 1,
                    skip_runtime_bounds_check_because="the offsets are clamped when they are made")
                for j in range(tiles):
                    t = g * TG + j
                    if j == 0:
                        dve.wait_ge(window_ready, g + 1)
                    dve.wait_ge(prod_ready, t + 1)
                    dve.wait_ge(prod_free, t + AHEAD)
                    w = agg[:, par, bass.ds(offs[j], SPAN), :].rearrange("p n r -> p (n r)")
                    dve.tensor_tensor(w, prod[j % AHEAD][:, 0:KEYS], w, ALU.add).then_inc(prod_free, 1)
                    if j + AHEAD < tiles or ahead:
                        make_onehot(t + AHEAD, j % AHEAD)
                return offs[TG]

            def sum_step(g, par):
                nxt = accumulate(g, par, TG, True)
                dve.wait_ge(prod_free, (g + 1) * TG + AHEAD)
                dve.wait_ge(agg_zeroed, g + 2)
                dve.tensor_copy(agg[:, 1 - par, 0, :],
                                agg[:, par, bass.ds(nxt, 1), :].rearrange("p n r -> p (n r)")
                                ).then_inc(window_ready, 1)

            with dve.Fori(0, CHECK_PAIR) as gg:
                for par in range(2):
                    sum_step(gg * 2 + par, par)

            dve.wait_ge(nxt_in, 48)
            dve.tensor_tensor(key[:, :, :], dst_i[:, :, :], nxt_i[:, :, :], ALU.subtract).then_inc(dve_step, 1)
            steps[0] += 1
            dve.wait_ge(dve_step, steps[0])
            link(dve.tensor_reduce(excess[:, 0:1], key[:, :, :].rearrange("p b e -> p (b e)"), AX.X, ALU.max))
            dve.tensor_scalar(excess[0:FULL, 2:3], first_i[0:FULL, TG:TG + 1], first_i[0:FULL, 0:1],
                              float(1 - P), ALU.subtract, ALU.add)
            dve.tensor_scalar(excess[0:FULL, 3:4], first_i[0:FULL, 0:1], float(P - N), None, ALU.add)
            link(dve.tensor_scalar(excess[:, 4:5], last_i[:, :], -1.0, float(N - P), ALU.mult, ALU.add))
            dve.tensor_reduce(excess_max[:, :], excess[:, :], AX.X, ALU.max).then_inc(excess_ready, 1)

            with dve.Fori(CHECK_PAIR, FULL // 2) as gg:
                for par in range(2):
                    sum_step(gg * 2 + par, par)
            accumulate(FULL, 0, LAST_TILES, False)
            dve.wait_ge(excess_turned, 1)
            link(dve.tensor_reduce(flag_f[0:1, :], flag_bank[0:1, 0:P], AX.X, ALU.max))
            dve.tensor_scalar(flag_i[0:1, :], flag_f[0:1, :], 0.0, None, ALU.is_gt).then_inc(flag_ready, 1)

            with general_path(dve):
                dve.wait_ge(general_x_in, 32)
                dve.tensor_tensor(xh[:, :, :], xh[:, :, :], bias_bc[:, None, :].to_broadcast([P, ROWS, D]),
                                  ALU.add).then_inc(general_biased, 1)
                dve.tensor_tensor(xr[0:REST, :], xr[0:REST, :], bias_bc[0:REST, :], ALU.add
                                  ).then_inc(general_biased, 1)
                dve.wait_ge(general_consts, 1)
                dve.tensor_scalar(before[:, :], places[:, :], part_f[:, :], None, ALU.is_lt
                                  ).then_inc(general_dve, 1)
                dve.wait_ge(general_dve, 1)

                def tile(t, n):
                    done = 6 * t + 1
                    for loaded in edges_in:
                        dve.wait_ge(loaded, 16 * (t + 1))
                    dve.tensor_copy(typ_f[0:n, :], typ_col[0:n, :])
                    dve.tensor_copy(dst_f[0:n, :], dst_col[0:n, :]).then_inc(general_dve, 1)
                    dve.wait_ge(general_dve, done + 1)
                    dve.tensor_scalar(same[0:n, 0:n], dst_row[0:n, 0:n], dst_f[0:n, :], None, ALU.is_equal)
                    dve.tensor_scalar(typ_onehot[0:n, :], keys_iota[0:n, 0, 0:R], typ_f[0:n, :], None, ALU.is_equal
                                      ).then_inc(general_dve, 1)
                    dve.wait_ge(general_dve, done + 2)
                    for r in range(R):
                        last = dve.tensor_scalar(picked[0:n, r, 0:n], same[0:n, 0:n], typ_onehot[0:n, r:r + 1],
                                                 None, ALU.mult)
                    last.then_inc(picked_ready, 1)
                    dve.tensor_tensor(twins[0:n, 0:n], same[0:n, 0:n], before[0:n, 0:n], ALU.mult
                                      ).then_inc(general_dve, 1)
                    dve.wait_ge(general_dve, done + 3)
                    dve.tensor_reduce(twins_f[0:n, :], twins[0:n, 0:n], AX.X, ALU.add).then_inc(general_dve, 1)
                    dve.wait_ge(general_dve, done + 4)
                    dve.tensor_scalar(skip_f[0:n, :], twins_f[0:n, :], 1.0, PAD, ALU.min, ALU.mult
                                      ).then_inc(general_dve, 1)
                    dve.wait_ge(general_dve, done + 5)
                    dve.tensor_tensor(target[0:n, :], skip_f[0:n, :], dst_f[0:n, :], ALU.add
                                      ).then_inc(target_ready, 1)
                    dve.sem_inc(general_dve, 1)
                    dve.wait_ge(rows_scattered, 16 * (t + 1))
                    dve.sem_inc(general_seen, 1)

                general_tiles(dve, tile)

        @block.tensor
        def _(pe):
            pe.wait_ge(consts_set, 1)

            def turn_over(tile, first):
                for k, bs in enumerate(batches()):
                    if k == 1 and first == 0:
                        pe.wait_ge(srcf_ready, 2)
                    if first + k >= 2:
                        pe.wait_ge(unturned, first + k - 1)
                    for i, b in enumerate(bs):
                        last = pe.transpose(turn[(first + k) % 2][:, i * P:(i + 1) * P], tile[:, b, :], ident[:, :])
                    last.then_inc(turned, 1)

            pe.wait_ge(srcf_ready, 1)
            turn_over(key, 0)
            pe.wait_ge(key_ready, 1)
            turn_over(key, len(batches()))
            pe.wait_ge(w_in, 32 * Q)
            for k in range(W_BANKS):
                if w_banks[k] in turn:
                    pe.wait_ge(unturned, 2 * len(batches()))
                n = DQ // W_BANKS
                for o in range(n):
                    last = pe.matmul(w_banks[k][:, o * Q * R:(o + 1) * Q * R], wt[:, :, k * n + o],
                                     wc_q[:, :, :].rearrange("p q r -> p (q r)"), start=True, stop=True)
                last.then_inc(w_turned, 1)
            pe.wait_ge(bias_in, 16)

            def mix_parts(g, par, tiles, rows, rows_done, rows_count, x_first=False):
                terms = ["x", "bias"] + list(range(R)) if x_first else list(range(R)) + ["bias", "x"]

                def part(term):
                    if term == "x":
                        pe.wait_ge(rows_done, rows_count)
                        left, right = ident[:, :], rows
                    elif term == "bias":
                        left, right = ident[:, :], bias_bc[:, :]
                    else:
                        if term == 0:
                            pe.wait_ge(prod_free, g * TG + tiles + AHEAD)
                        left, right = agg[:, par, 0:P, term], W[:, term, :]
                    product = pe.matmul(mix[par][:, 0:D], left, right,
                                        start=(term == terms[0]), stop=(term == terms[-1]))
                    if term == terms[-1]:
                        product.then_inc(mixed, 1)

                return [lambda term=term: part(term) for term in terms]

            def products(g, tiles, early, parts=()):
                parts = list(parts)
                for j in range(tiles):
                    t = g * TG + j
                    if j < TABLE_TILES:
                        pe.wait_ge(gathered[j], (g + 1) * 16)
                    elif not early:
                        pe.wait_ge(gathered[j], (g + (1 - EARLY_GROUPS)) * 16)
                    elif j == TABLE_TILES:
                        pe.wait_ge(early_placed, g + 1)
                    pe.wait_ge(onehot_ready, t + 1)
                    pe.wait_ge(prod_free, t + 1)
                    pe.matmul(prod[j % AHEAD][:, 0:KEYS], G[:, j, :], onehot[:, j % AHEAD, :],
                              start=True, stop=True).then_inc(prod_ready, 1)
                    if j >= MIX_FROM:
                        for part in parts[:MIX_EACH]:
                            part()
                        parts = parts[MIX_EACH:]
                assert not parts

            def mix_full(g, par):
                return mix_parts(g, par, TG, x_t[:, par, :], xt_in[par], (g - par) * 8 + 16)

            products(0, TG, True)
            pe.wait_ge(w_ready, W_BANKS)
            for start, groups, early in RUNS:
                with pe.Fori(0, groups // 2) as gg:
                    for i in range(2):
                        g = gg * 2 + (start + i)
                        products(g, TG, early, mix_full(g - 1, (start + i - 1) % 2))
            products(FULL - 1, TG, False, mix_full(FULL - 2, 0))
            pe.wait_ge(excess_ready, 1)
            pe.transpose(flag_bank[0:1, 0:P], excess_max[:, :], ident[:, :]).then_inc(excess_turned, 1)
            products(FULL, LAST_TILES, False, mix_full(FULL - 1, 1))
            for part in mix_parts(FULL, 0, LAST_TILES, x_last[:, :], x_last_in, 16, x_first=True):
                part()

            with general_path(pe):
                def tile(t, n):
                    pe.wait_ge(picked_ready, t + 1)
                    pe.wait_ge(rows_gathered[0], 16 * (t + 1))
                    for k in range(R // 4):
                        last = pe.matmul(sum_banks[k][:, :].rearrange("p (r e) -> p r e", e=P)[:, :, 0:n],
                                         h_rows[0:n, :], picked[0:n, 4 * k:4 * k + 4, 0:n], start=True, stop=True)
                    last.then_inc(sums_ready, 1)
                    pe.wait_ge(rows_gathered[1], 16 * (t + 1))
                    pe.matmul(mix[0][0:n, 0:D], ident[0:n, 0:n], out_rows[0:n, :], start=True, stop=False)
                    pe.wait_ge(sums_moved, t + 1)
                    for r in range(R):
                        last = pe.matmul(mix[0][0:n, 0:D], sums[:, r, 0:n], W[:, r, :],
                                         start=False, stop=(r == R - 1))
                    last.then_inc(new_rows_ready, 1)

                general_tiles(pe, tile)


_INS = ['x', 'src', 'dst', 'edge_type_16', 'L0_gnn_weight', 'L0_gnn_w_comp', 'L0_gnn_h_bias']


def kernel(**inputs):
    import numpy as _np
    import concourse.bacc as _bacc
    from concourse import mybir as _mybir
    from concourse.bass_utils import run_bass_kernel_spmd as _run

    nc = _bacc.Bacc("TRN2", target_bir_lowering=False, num_devices=1)
    arrays, args = {}, []
    for name in _INS:
        a = _np.ascontiguousarray(inputs[name])
        arrays[f"in_{name}_dram"] = a
        args.append(nc.dram_tensor(f"in_{name}_dram", a.shape, _mybir.dt.from_np(a.dtype), kind="ExternalInput").ap())
    out = nc.dram_tensor("out_0_dram", inputs["x"].shape, _mybir.dt.float32, kind="ExternalOutput").ap()
    gnn_kernel(nc, *args, out)
    return _run(nc, [arrays], core_ids=[0]).results[0]["out_0_dram"]
```
